# Optimizing a Trainium2 kernel written in Bass

```python
import numpy as np
import jax
import jax.numpy as jnp

def _softmax(x, axis=-1):
    return jax.nn.softmax(x, axis=axis)

def _gelu(x):
    return jax.nn.gelu(x, approximate=True)

def _silu(x):
    return jax.nn.silu(x)

def _sigmoid(x):
    return jax.nn.sigmoid(x)

def _layernorm(x, axis=-1, eps=1e-05):
    m = jnp.mean(x, axis=axis, keepdims=True)
    v = jnp.var(x, axis=axis, keepdims=True)
    return (x - m) / jnp.sqrt(v + eps)

def _scatter_add(tgt, idx, src, axis=0):
    return tgt.at[idx].add(src)

def _segment_sum(src, seg, n):
    return jax.ops.segment_sum(src, seg, n)
kernel_name = 'mk_cond_resid_d2_seqx_r4_b64c59'

def setup_inputs(seed: int=0):
    np.random.seed(seed)
    _w = jnp.asarray

    def _rec_inputs():
        import jax
        import jax.numpy as jnp
        _rk = jax.random.key(seed)
        x = -0.0001546 + 1 * jax.random.normal(jax.random.fold_in(_rk, 1), (8, 256, 256), jnp.float32)
        _lenS = 256 - jax.random.randint(jax.random.fold_in(_rk, 7), (8,), 0, max(1, 256 // 4) + 1, jnp.int32)
        _lenS2 = 256 - jax.random.randint(jax.random.fold_in(_rk, 8), (8,), 0, max(1, 256 // 4) + 1, jnp.int32)
        itok_B_1_98 = jax.random.randint(jax.random.fold_in(_rk, 11), (8,), 1, 99, jnp.int32)
        itok_B_0_2 = jax.random.randint(jax.random.fold_in(_rk, 12), (8,), 0, 3, jnp.int32)
        return (x, itok_B_1_98, itok_B_0_2)
    x, itok_B_1_98, itok_B_0_2 = _rec_inputs()

    def _L0_cond_setup():
        import jax, jax.numpy as jnp
        import numpy as np
        B = 128
        D = 256
        K = 100
        key = jax.random.key(seed)
        kx, kt, ks = jax.random.split(key, 3)
        x = jax.random.normal(kx, (B, D, D), dtype=jnp.float32)
        T = jax.random.normal(kt, (K, D, D), dtype=jnp.float32)
        fwd_steps = jax.random.randint(ks, (B,), 1, K + 1, dtype=jnp.int64)
        return {'x': x, 'fwd_steps': fwd_steps, 'T': T}
    _L0_cond_all = _L0_cond_setup()
    _L0_cond_in = {k: v for k, v in _L0_cond_all.items() if k in ('T',)}
    del _L0_cond_all

    def _L1_cond_setup():
        import jax, jax.numpy as jnp
        import numpy as np
        D_MODEL = 256
        D_FF = 1024
        N_EXPERTS = 5
        BATCH = 8
        SEQ = 512

        def _gated_ffn(x, wi0, wi1, wo):
            g = jax.nn.gelu(x @ wi0, approximate=True)
            l = x @ wi1
            return g * l @ wo
        key = jax.random.key(seed)
        ks = jax.random.split(key, 12)
        s = 0.02
        inp = {'hidden_states': jax.random.normal(ks[0], (BATCH, SEQ, D_MODEL), jnp.float32), 'type_label': jax.random.randint(ks[1], (BATCH,), 0, N_EXPERTS, jnp.int32), 'Wi0': jax.random.normal(ks[2], (N_EXPERTS, D_MODEL, D_FF), jnp.float32) * s, 'Wi1': jax.random.normal(ks[3], (N_EXPERTS, D_MODEL, D_FF), jnp.float32) * s, 'Wo': jax.random.normal(ks[4], (N_EXPERTS, D_FF, D_MODEL), jnp.float32) * s, 'sWi0': jax.random.normal(ks[5], (D_MODEL, D_FF), jnp.float32) * s, 'sWi1': jax.random.normal(ks[6], (D_MODEL, D_FF), jnp.float32) * s, 'sWo': jax.random.normal(ks[7], (D_FF, D_MODEL), jnp.float32) * s, 'g0': jax.random.normal(ks[8], (2 * D_MODEL, D_MODEL), jnp.float32) * s, 'g1': jax.random.normal(ks[9], (D_MODEL, 2), jnp.float32) * s}
        return inp
    _L1_cond_all = _L1_cond_setup()
    _L1_cond_in = {k: v for k, v in _L1_cond_all.items() if k in ('Wi0', 'Wi1', 'Wo', 'sWi0', 'sWi1', 'sWo', 'g0', 'g1')}
    del _L1_cond_all
    return {'x': x, 'itok_B_1_98': itok_B_1_98, 'itok_B_0_2': itok_B_0_2, 'L0_cond_T': _L0_cond_in['T'], 'L1_cond_Wi0': _L1_cond_in['Wi0'], 'L1_cond_Wi1': _L1_cond_in['Wi1'], 'L1_cond_Wo': _L1_cond_in['Wo'], 'L1_cond_sWi0': _L1_cond_in['sWi0'], 'L1_cond_sWi1': _L1_cond_in['sWi1'], 'L1_cond_sWo': _L1_cond_in['sWo'], 'L1_cond_g0': _L1_cond_in['g0'], 'L1_cond_g1': _L1_cond_in['g1']}

def reference(x, itok_B_1_98, itok_B_0_2, L0_cond_T, L1_cond_Wi0, L1_cond_Wi1, L1_cond_Wo, L1_cond_sWi0, L1_cond_sWi1, L1_cond_sWo, L1_cond_g0, L1_cond_g1):
    import jax
    import jax.numpy as jnp

    def _L0_cond_ref(x, fwd_steps, T):
        import jax, jax.numpy as jnp
        import numpy as np
        B = 128
        D = 256
        K = 100
        Tb = T[fwd_steps - 1]
        return jnp.einsum('bij,bjk->bik', Tb, x)

    def _L1_cond_ref(hidden_states, type_label, Wi0, Wi1, Wo, sWi0, sWi1, sWo, g0, g1):
        import jax, jax.numpy as jnp
        import numpy as np
        D_MODEL = 256
        D_FF = 1024
        N_EXPERTS = 5
        BATCH = 8
        SEQ = 512

        def _gated_ffn(x, wi0, wi1, wo):
            g = jax.nn.gelu(x @ wi0, approximate=True)
            l = x @ wi1
            return g * l @ wo
        share_out = _gated_ffn(hidden_states, sWi0, sWi1, sWo)
        wi0 = Wi0[type_label]
        wi1 = Wi1[type_label]
        wo = Wo[type_label]
        hg = jax.nn.gelu(jnp.einsum('bsd,bdf->bsf', hidden_states, wi0), approximate=True)
        hl = jnp.einsum('bsd,bdf->bsf', hidden_states, wi1)
        expert_out = jnp.einsum('bsf,bfd->bsd', hg * hl, wo)
        gate_in = jnp.concatenate([expert_out[:, 0], share_out[:, 0]], axis=-1)
        weights = jax.nn.softmax(jax.nn.relu(gate_in @ g0) @ g1, axis=-1)
        w0 = weights[:, 0][:, None, None]
        w1 = weights[:, 1][:, None, None]
        return expert_out * w0 + share_out * w1
    x = x + _L0_cond_ref(x, itok_B_1_98, L0_cond_T)
    x = x + _L1_cond_ref(x, itok_B_0_2, L1_cond_Wi0, L1_cond_Wi1, L1_cond_Wo, L1_cond_sWi0, L1_cond_sWi1, L1_cond_sWo, L1_cond_g0, L1_cond_g1)
    return x

_drawn_inputs = setup_inputs


def setup_inputs(seed=0):
    import zlib

    import numpy as np

    out = dict(_drawn_inputs(seed))
    spreads = {}
    factors = {}
    for name, (base, spread) in spreads.items():
        noise = np.random.default_rng([zlib.crc32(name.encode()), seed]).standard_normal(out[name].shape)
        drawn = base * np.exp(spread * noise) if base else spread * noise
        out[name] = jnp.asarray(drawn.astype(out[name].dtype))
    for name, factor in factors.items():
        out[name] = (out[name] * factor).astype(out[name].dtype)
    return out
```

```python
import concourse.bass as bass
from concourse import mybir
from contextlib import ExitStack

FP32 = mybir.dt.float32
FP32R = mybir.dt.float32r
INT32 = mybir.dt.int32
ALU = mybir.AluOpType
ACT = mybir.ActivationFunctionType
AXIS = mybir.AxisListType


def conditioned_residual_kernel(nc, x, itok_t, itok_e, T, Wi0, Wi1, Wo, sWi0, sWi1, sWo, g0, g1, out):
    P = 128
    B, S, D = x.shape
    F = sWi0.shape[1]
    K_STEPS, N_EXPERTS = T.shape[0], Wi0.shape[0]
    DC, SC, FC = D // P, S // P, F // P
    HALF = F // 2
    FPH = FC // 2
    FPT = 2
    TPN = FC // FPT
    TILES = 2 * TPN
    SHARED, EXPERT = 0, 1
    HI, LO = 0, 1
    PASSES = ((HI, HI), (HI, LO), (LO, HI))
    PIECES = 6
    WI_HALF0, WI_HALF1, WO = (0, 1), (2, 3), (4, 5)

    with ExitStack() as ctx:
        def sb(name, shape, dt=FP32):
            return ctx.enter_context(nc.sbuf_tensor(name, shape, dt))

        def ps(name, shape):
            return ctx.enter_context(nc.psum_tensor(name, shape, FP32))

        def sem(name):
            return ctx.enter_context(nc.semaphore(name))

        steps_sb = sb("steps_sb", [1, B], INT32)
        labels_sb = sb("labels_sb", [1, B], INT32)
        ident = sb("ident", [P, P])
        ones = sb("ones", [P, P])
        g0_sb = sb("g0_sb", [P, 2 * DC, D])
        g1_sb = sb("g1_sb", [P, DC, 2])
        raw = [sb(f"raw{k}", [P, 1024]) for k in range(PIECES)]
        wi_split = [sb(f"wi{m}_split", [P, 2, 2, DC, F], FP32R) for m in range(2)]
        wo_split = sb("wo_split", [P, 2, 2, FC, D], FP32R)
        T_sb = sb("T_sb", [P, SC, S])
        x_sb = sb("x_sb", [P, SC, D])
        x_split = sb("x_split", [P, 2, SC, D], FP32R)
        tT_split = sb("tT_split", [P, 2, SC, S], FP32R)
        h_sb = sb("h_sb", [P, SC, D])
        h_keep = sb("h_keep", [P, SC, D])
        hT_split = sb("hT_split", [P, 2, DC, S], FP32R)
        prod = sb("prod", [P, 2, FPT, S])
        prod_split = sb("prod_split", [P, 2, 2, FC, S], FP32R)
        gate_row = sb("gate_row", [1, 2 * D])
        gateT = sb("gateT", [P, 2 * DC])
        relu_bc = sb("relu_bc", [P, DC, P])
        lmax = sb("lmax", [P, 1])
        lshift = sb("lshift", [P, 2])
        lexp = sb("lexp", [P, 2])
        lsum = sb("lsum", [P, 1])
        lrec = sb("lrec", [P, 1])
        wgt = sb("wgt", [P, 2])
        part = sb("part", [P, SC, D])
        out_sb = sb("out_sb", [P, SC, D])

        up_gate = [ps(f"up_gate{i}", [P, FPT, S]) for i in range(2)]
        up_lin = [ps(f"up_lin{i}", [P, FPT, S]) for i in range(2)]
        down = [ps(f"down{c}", [P, 2, D]) for c in range(SC)]
        front = ps("front", [P, 2, 256])
        mini = ps("mini", [P, 512])
        mini_gT, mini_z, mini_l = mini[:, 0:2 * DC], mini[:, 8:8 + DC], mini[:, 16:18]

        steps_landed, labels_landed = sem("steps_landed"), sem("labels_landed")
        T_landed, x_landed = sem("T_landed"), sem("x_landed")
        g0_landed, g1_landed = sem("g0_landed"), sem("g1_landed")
        raw_landed = [sem(f"raw{k}_landed") for k in range(PIECES)]
        hi_done = [sem(f"hi{k}_done") for k in range(PIECES)]
        piece_split = [sem(f"piece{k}_split") for k in range(PIECES)]
        ones_made, ident_made, ident_zeroed = sem("ones_made"), sem("ident_made"), sem("ident_zeroed")
        tT_ready, x_hi_done, tT_hi_done = sem("tT_ready"), sem("x_hi_done"), sem("tT_hi_done")
        x_lo_done, tT_lo_done = sem("x_lo_done"), sem("tT_lo_done")
        h_ready, h_done, h_kept = sem("h_ready"), sem("h_done"), sem("h_kept")
        hT_ready, hT_hi_done, hT_lo_done = sem("hT_ready"), sem("hT_hi_done"), sem("hT_lo_done")
        gate_ready, lin_ready = sem("gate_ready"), sem("lin_ready")
        gelu_done, prod_done = sem("gelu_done"), sem("prod_done")
        prod_hi_done, prod_lo_done = sem("prod_hi_done"), sem("prod_lo_done")
        down_ready = [sem(f"down{c}_ready") for c in range(SC)]
        row_done, gT_ready, gT_done = sem("row_done"), sem("gT_ready"), sem("gT_done")
        z_ready, relu_done, logits_ready = sem("z_ready"), sem("relu_done"), sem("logits_ready")
        max_done, shift_done, exp_done = sem("max_done"), sem("shift_done"), sem("exp_done")
        rec_done, wgt_done, part_done = sem("rec_done"), sem("wgt_done"), sem("part_done")
        final_done = [sem(f"final{c}_done") for c in range(SC)]
        out_stored = [sem(f"out{c}_stored") for c in range(SC)]

        def wait(eng, semaphore, value):
            if not isinstance(value, int) or value > 0:
                eng.wait_ge(semaphore, value)

        def piece_dst(n_is_shared, k, part_):
            net = SHARED if n_is_shared else EXPERT
            if k in WO:
                c = (k - WO[0]) * FPH
                return wo_split[:, net, part_, c:c + FPH, :]
            return wi_split[k % 2][:, net, part_, :, (k // 2) * HALF:(k // 2 + 1) * HALF]

        def raw_view(k):
            a = FPH if k in WO else DC
            return raw[k][:, :].rearrange("p (a n) -> p a n", a=a)

        def pieces_before(b_kind, b):
            if b_kind == "first":
                return {0: [(0, 0), (0, 1)], 2: [(0, 2), (0, 3)], 4: [(1, 0), (1, 1)], 5: [(0, 4)],
                        6: [(1, 2), (1, 3)], 7: [(0, 5), (1, 4), (1, 5)], TILES: [(2, 0), (2, 1), (2, 2), (2, 3)]}
            sets = {1: [(b + 1, 4)], 2: [(b + 1, 5)]}
            if b_kind == "middle":
                sets[7] = [(b + 2, 0), (b + 2, 1)]
                sets[TILES] = [(b + 2, 2), (b + 2, 3)]
            return sets

        def is_shared(n):
            return isinstance(n, int) and n == 0

        def over_batches(eng, body):
            body("first", 0)
            with eng.Fori(1, B - 1) as b:
                body("middle", b)
            body("last", B - 1)

        block = ctx.enter_context(nc.Block())

        @block.sync
        def _(sp):
            sp.dma_start(steps_sb[:, :], itok_t.rearrange("(o b) -> o b", o=1)).then_inc(steps_landed, 16)
            sp.dma_start(labels_sb[:, :], itok_e.rearrange("(o b) -> o b", o=1)).then_inc(labels_landed, 16)

            def load_front(b):
                if not (isinstance(b, int) and b == 0):
                    sp.wait_ge(h_done, b)
                sp.dma_start(x_sb[:, :, :], x[bass.ds(b, 1), :, :].rearrange("o (c p) d -> p (o c) d", p=P)
                             ).then_inc(x_landed, 16)
                step = sp.value_load(steps_sb[0:1, bass.ds(b, 1)], min_val=1, max_val=K_STEPS)
                sp.dma_start(T_sb[:, :, :], T[bass.ds(step - 1, 1), :, :].rearrange("o (c p) s -> p (o c) s", p=P)
                             ).then_inc(T_landed, 16)

            def load_piece(n, k, label=None):
                wait(sp, piece_split[k], n)
                if is_shared(n):
                    src = (sWi0, sWi1)[k % 2] if k not in WO else sWo
                else:
                    w = (Wi0, Wi1)[k % 2] if k not in WO else Wo
                    src = w[bass.ds(label, 1), :, :].rearrange("o r c -> (o r) c")
                if k in WO:
                    h = k - WO[0]
                    src = src[h * HALF:(h + 1) * HALF, :].rearrange("(c p) n -> p c n", p=P)
                else:
                    h = k // 2
                    src = src[:, h * HALF:(h + 1) * HALF].rearrange("(c p) n -> p c n", p=P)
                sp.dma_start(raw_view(k), src).then_inc(raw_landed[k], 16)

            def expert_of(b):
                return sp.value_load(labels_sb[0:1, bass.ds(b, 1)], min_val=0, max_val=N_EXPERTS - 1)

            sp.wait_ge(steps_landed, 16)
            load_front(0)
            for k in range(PIECES - 2):
                load_piece(0, k)
            sp.wait_ge(labels_landed, 16)
            label = expert_of(0)
            load_piece(1, 0, label)
            load_piece(1, 1, label)
            load_piece(0, 4)
            load_piece(1, 2, label)
            load_piece(1, 3, label)
            load_front(1)
            load_piece(0, 5)
            load_piece(1, 4, label)
            load_piece(1, 5, label)
            sp.dma_start(g0_sb[:, :, :], g0.rearrange("(c p) n -> p c n", p=P)).then_inc(g0_landed, 16)
            sp.dma_start(g1_sb[:, :, :], g1.rearrange("(c p) n -> p c n", p=P)).then_inc(g1_landed, 16)

            def load_expert(b):
                label = expert_of(b)
                for k in range(PIECES):
                    load_piece(b + 1, k, label)

            def store(b):
                for c in range(SC):
                    sp.wait_ge(final_done[c], b + 1)
                    sp.dma_start(out[bass.ds(b, 1), c * P:(c + 1) * P, :].rearrange("o p d -> p (o d)"),
                                 out_sb[:, c, :]).then_inc(out_stored[c], 16)

            with sp.Fori(0, B - 2) as b:
                load_expert(b + 1)
                load_front(b + 2)
                store(b)
            load_expert(B - 1)
            store(B - 2)
            store(B - 1)
            for c in range(SC):
                sp.wait_ge(out_stored[c], 16 * B)

        @block.gpsimd
        def _(pool):
            nc.gpsimd.memset(ones[:, :], 1.0).then_inc(ones_made, 1)
            nc.gpsimd.memset(ident[:, :], 0.0).then_inc(ident_zeroed, 1)
            pool.wait_ge(ident_zeroed, 1)
            nc.gpsimd.affine_select(out=ident[:, :], in_=ident[:, :], compare_op=ALU.not_equal, fill=1.0, base=0,
                                    pattern=[[-1, P]], channel_multiplier=1).then_inc(ident_made, 1)

        @block.scalar
        def _(act):
            def x_and_T_hi(b):
                act.wait_ge(x_landed, 16 * (b + 1))
                wait(act, h_ready, b)
                nc.scalar.copy(x_split[:, HI], x_sb[:, :, :]).then_inc(x_hi_done, 1)
                act.wait_ge(tT_ready, b + 1)
                nc.scalar.copy(tT_split[:, HI], front[:, :, :]).then_inc(tT_hi_done, 1)

            def keep_h(b):
                act.wait_ge(h_done, b + 1)
                wait(act, final_done[SC - 1], b)
                nc.scalar.copy(h_keep[:, :, :], h_sb[:, :, :]).then_inc(h_kept, 1)

            def hT_hi(b):
                act.wait_ge(hT_ready, b + 1)
                nc.scalar.copy(hT_split[:, HI], front[:, :, :]).then_inc(hT_hi_done, 1)

            def piece_hi(n, k):
                act.wait_ge(raw_landed[k], 16 * (n + 1))
                if k in WO:
                    wait(act, down_ready[SC - 1], n - 1)
                elif not isinstance(n, int) or n > 1:
                    act.wait_ge(lin_ready, TILES * (n - 2) + TPN + (k // 2 + 1) * TPN // 2)
                nc.scalar.copy(piece_dst(is_shared(n), k, HI), raw_view(k)).then_inc(hi_done[k], 1)

            def prod_hi(b, t):
                net, tt = divmod(t, TPN)
                act.wait_ge(prod_done, TILES * b + t + 1)
                nc.scalar.copy(prod_split[:, net, HI, tt * FPT:(tt + 1) * FPT, :], prod[:, t % 2]
                               ).then_inc(prod_hi_done, 1)

            def batch(kind, b):
                sets = pieces_before(kind, b)
                for t in range(TILES):
                    for n, k in sets.get(t, ()):
                        piece_hi(n, k)
                    act.wait_ge(gate_ready, TILES * b + t + 1)
                    wait(act, prod_lo_done, TILES * b + t - 1)
                    nc.scalar.activation(prod[:, t % 2], up_gate[t % 2][:, :, :], ACT.Gelu_apprx_tanh
                                         ).then_inc(gelu_done, 1)
                    if t > 0:
                        prod_hi(b, t - 1)
                    if t == 1:
                        keep_h(b)
                    if t == 5 and kind != "last":
                        x_and_T_hi(b + 1)
                prod_hi(b, TILES - 1)
                for n, k in sets.get(TILES, ()):
                    piece_hi(n, k)
                act.wait_ge(down_ready[0], b + 1)
                nc.scalar.copy(gate_row[0:1, :], down[0][0:1, :, :].rearrange("p a d -> p (a d)")
                               ).then_inc(row_done, 1)
                if kind != "last":
                    hT_hi(b + 1)
                act.wait_ge(gT_ready, b + 1)
                nc.scalar.copy(gateT[:, :], mini_gT).then_inc(gT_done, 1)
                act.wait_ge(shift_done, b + 1)
                nc.scalar.activation(lexp[:, :], lshift[:, :], ACT.Exp, accum_out=lsum[:, :]).then_inc(exp_done, 1)

            x_and_T_hi(0)
            hT_hi(0)
            over_batches(act, batch)

        @block.vector
        def _(dve):
            def f32(ap):
                return ap.bitcast(FP32)

            def x_and_T_lo(b):
                dve.wait_ge(x_hi_done, b + 1)
                nc.vector.tensor_tensor(x_split[:, LO], x_sb[:, :, :], f32(x_split[:, HI]), ALU.subtract
                                        ).then_inc(x_lo_done, 1)
                dve.wait_ge(tT_hi_done, b + 1)
                nc.vector.tensor_tensor(tT_split[:, LO], front[:, :, :], f32(tT_split[:, HI]), ALU.subtract
                                        ).then_inc(tT_lo_done, 1)

            def h_add(b):
                dve.wait_ge(h_ready, b + 1)
                wait(dve, h_kept, b)
                nc.vector.tensor_tensor(h_sb[:, :, :], front[:, :, :], x_sb[:, :, :], ALU.add).then_inc(h_done, 1)

            def hT_lo(b):
                dve.wait_ge(hT_hi_done, b + 1)
                nc.vector.tensor_tensor(hT_split[:, LO], front[:, :, :], f32(hT_split[:, HI]), ALU.subtract
                                        ).then_inc(hT_lo_done, 1)

            def piece_lo(n, k):
                dve.wait_ge(hi_done[k], n + 1)
                nc.vector.tensor_tensor(piece_dst(is_shared(n), k, LO), raw_view(k),
                                        f32(piece_dst(is_shared(n), k, HI)), ALU.subtract).then_inc(piece_split[k], 1)

            def prod_lo(b, t):
                net, tt = divmod(t, TPN)
                fs = slice(tt * FPT, (tt + 1) * FPT)
                dve.wait_ge(prod_hi_done, TILES * b + t + 1)
                nc.vector.tensor_tensor(prod_split[:, net, LO, fs, :], prod[:, t % 2],
                                        f32(prod_split[:, net, HI, fs, :]), ALU.subtract).then_inc(prod_lo_done, 1)

            def batch(kind, b):
                sets = pieces_before(kind, b)
                for t in range(TILES):
                    for n, k in sets.get(t, ()):
                        piece_lo(n, k)
                    dve.wait_ge(gelu_done, TILES * b + t + 1)
                    dve.wait_ge(lin_ready, TILES * b + t + 1)
                    nc.vector.tensor_tensor(prod[:, t % 2], up_lin[t % 2][:, :, :], prod[:, t % 2], ALU.mult
                                            ).then_inc(prod_done, 1)
                    if t > 0:
                        prod_lo(b, t - 1)
                    if t == 5 and kind != "last":
                        x_and_T_lo(b + 1)
                prod_lo(b, TILES - 1)
                if kind != "last":
                    h_add(b + 1)
                for n, k in sets.get(TILES, ()):
                    piece_lo(n, k)
                if kind != "last":
                    hT_lo(b + 1)
                dve.wait_ge(z_ready, b + 1)
                if kind == "first":
                    dve.wait_ge(ones_made, 1)
                for m in range(DC):
                    nc.vector.tensor_scalar(relu_bc[:, m, :], ones[:, :], mini_z[:, m:m + 1], 0.0, ALU.mult, ALU.max
                                            ).then_inc(relu_done, 1)
                dve.wait_ge(logits_ready, b + 1)
                nc.vector.reduce_max(lmax[:, :], mini_l, AXIS.X).then_inc(max_done, 1)
                dve.wait_ge(max_done, b + 1)
                nc.vector.tensor_scalar(lshift[:, :], mini_l, lmax[:, :], None, ALU.subtract).then_inc(shift_done, 1)
                dve.wait_ge(exp_done, b + 1)
                nc.vector.reciprocal(lrec[:, :], lsum[:, :]).then_inc(rec_done, 1)
                dve.wait_ge(rec_done, b + 1)
                nc.vector.tensor_scalar(wgt[:, :], lexp[:, :], lrec[:, :], None, ALU.mult).then_inc(wgt_done, 1)
                dve.wait_ge(wgt_done, b + 1)
                dve.wait_ge(h_kept, b + 1)
                for c in range(SC):
                    dve.wait_ge(down_ready[c], b + 1)
                    wait(dve, out_stored[c], 16 * b)
                    nc.vector.scalar_tensor_tensor(out=part[:, c, :], in0=down[c][:, 0, :], scalar=wgt[:, 0:1],
                                                   in1=h_keep[:, c, :], op0=ALU.mult, op1=ALU.add
                                                   ).then_inc(part_done, 1)
                    dve.wait_ge(part_done, SC * b + c + 1)
                    nc.vector.scalar_tensor_tensor(out=out_sb[:, c, :], in0=down[c][:, 1, :], scalar=wgt[:, 1:2],
                                                   in1=part[:, c, :], op0=ALU.mult, op1=ALU.add
                                                   ).then_inc(final_done[c], 1)

            x_and_T_lo(0)
            h_add(0)
            hT_lo(0)
            over_batches(dve, batch)

        @block.tensor
        def _(pe):
            def transposes(src):
                for r in range(2):
                    for c in range(2):
                        last = nc.tensor.transpose(front[:, c, r * P:(r + 1) * P], src[:, r, c * P:(c + 1) * P],
                                                   ident[:, :])
                return last

            def T_transposed(b):
                pe.wait_ge(T_landed, 16 * (b + 1))
                wait(pe, hT_lo_done, b)
                transposes(T_sb).then_inc(tT_ready, 1)

            def h_product(b):
                pe.wait_ge(x_lo_done, b + 1)
                pe.wait_ge(tT_lo_done, b + 1)
                for c in range(SC):
                    terms = [(j, l, r) for j in range(SC) for l, r in PASSES]
                    for i, (j, l, r) in enumerate(terms):
                        last = nc.tensor.matmul(front[:, c, :], tT_split[:, l, j, c * P:(c + 1) * P],
                                                x_split[:, r, j, :], start=i == 0, stop=i == len(terms) - 1)
                last.then_inc(h_ready, 1)

            def h_transposed(b):
                pe.wait_ge(h_done, b + 1)
                transposes(h_sb).then_inc(hT_ready, 1)

            def up_tile(b, t):
                net, tt = divmod(t, TPN)
                wait(pe, prod_done, TILES * b + t - 1)
                for m, (bank, ready) in enumerate(((up_gate[t % 2], gate_ready), (up_lin[t % 2], lin_ready))):
                    for j in range(FPT):
                        f = tt * FPT + j
                        terms = [(c, l, r) for c in range(DC) for l, r in PASSES]
                        for i, (c, l, r) in enumerate(terms):
                            last = nc.tensor.matmul(bank[:, j, :], wi_split[m][:, net, l, c, f * P:(f + 1) * P],
                                                    hT_split[:, r, c, :], start=i == 0, stop=i == len(terms) - 1)
                    last.then_inc(ready, 1)

            def down_chunks(c, net, fs, first, final):
                col = {EXPERT: 0, SHARED: 1}[net]
                terms = [(f, l, r) for f in fs for l, r in PASSES]
                for i, (f, l, r) in enumerate(terms):
                    last = nc.tensor.matmul(down[c][:, col, :], prod_split[:, net, l, f, c * P:(c + 1) * P],
                                            wo_split[:, net, r, f, :], start=first and i == 0,
                                            stop=final and i == len(terms) - 1)
                return last

            def batch(kind, b):
                pe.wait_ge(hT_lo_done, b + 1)
                for t in range(TILES):
                    net = t // TPN
                    if t % TPN in (0, TPN // 2):
                        half = (t % TPN) // (TPN // 2)
                        for k in (WI_HALF0, WI_HALF1)[half]:
                            if net == EXPERT:
                                pe.wait_ge(piece_split[k], b + 2)
                            elif kind == "first":
                                pe.wait_ge(piece_split[k], 1)
                    up_tile(b, t)
                    if t == 5 and kind != "last":
                        T_transposed(b + 1)
                if kind != "last":
                    h_product(b + 1)
                if kind == "first":
                    for k in WO:
                        pe.wait_ge(piece_split[k], 1)
                pe.wait_ge(prod_lo_done, TILES * b + TPN)
                wait(pe, final_done[0], b)
                every, low, high = range(FC), range(FPH), range(FPH, FC)
                down_chunks(0, SHARED, every, True, True)
                pe.wait_ge(prod_lo_done, TILES * (b + 1))
                for k in WO:
                    pe.wait_ge(piece_split[k], b + 2)
                down_chunks(0, EXPERT, every, True, True).then_inc(down_ready[0], 1)
                if kind != "last":
                    h_transposed(b + 1)
                wait(pe, final_done[1], b)
                down_chunks(1, SHARED, low, True, False)
                pe.wait_ge(row_done, b + 1)
                for c in range(2 * DC):
                    last = nc.tensor.matmul(mini_gT[:, c:c + 1], gate_row[0:1, c * P:(c + 1) * P],
                                            ident[0:1, 0:1], start=True, stop=True)
                last.then_inc(gT_ready, 1)
                down_chunks(1, SHARED, high, False, True)
                pe.wait_ge(gT_done, b + 1)
                if kind == "first":
                    pe.wait_ge(g0_landed, 16)
                    pe.wait_ge(g1_landed, 16)
                for m in range(DC):
                    for c in range(2 * DC):
                        last = nc.tensor.matmul(mini_z[:, m:m + 1], g0_sb[:, c, m * P:(m + 1) * P],
                                                gateT[:, c:c + 1], start=c == 0, stop=c == 2 * DC - 1)
                last.then_inc(z_ready, 1)
                down_chunks(1, EXPERT, low, True, False)
                pe.wait_ge(relu_done, DC * (b + 1))
                for m in range(DC):
                    last = nc.tensor.matmul(mini_l, relu_bc[:, m, :], g1_sb[:, m, :], start=m == 0, stop=m == DC - 1)
                last.then_inc(logits_ready, 1)
                down_chunks(1, EXPERT, high, False, True).then_inc(down_ready[1], 1)

            pe.wait_ge(ident_made, 1)
            T_transposed(0)
            h_product(0)
            h_transposed(0)
            over_batches(pe, batch)


_INS = ['x', 'itok_B_1_98', 'itok_B_0_2', 'L0_cond_T', 'L1_cond_Wi0', 'L1_cond_Wi1', 'L1_cond_Wo',
        'L1_cond_sWi0', 'L1_cond_sWi1', 'L1_cond_sWo', 'L1_cond_g0', 'L1_cond_g1']


def kernel(**inputs):
    import numpy as _np
    import concourse.bacc as _bacc
    from concourse import mybir as _mybir
    from concourse.bass_utils import run_bass_kernel_spmd as _run

    nc = _bacc.Bacc("TRN2", target_bir_lowering=False, num_devices=1)
    arrays, args = {}, []
    for name in _INS:
        a = _np.ascontiguousarray(inputs[name])
        arrays[f"in_{name}_dram"] = a
        args.append(nc.dram_tensor(f"in_{name}_dram", a.shape, _mybir.dt.from_np(a.dtype), kind="ExternalInput").ap())
    out = nc.dram_tensor("out_0_dram", inputs['x'].shape, _mybir.dt.float32, kind="ExternalOutput").ap()
    conditioned_residual_kernel(nc, *args, out)
    r = _run(nc, [arrays], core_ids=[0])
    return r.results[0]["out_0_dram"]
```

```python
import concourse.bass as bass
from concourse import mybir
from contextlib import ExitStack

FP32 = mybir.dt.float32
FP32R = mybir.dt.float32r
INT32 = mybir.dt.int32
ALU = mybir.AluOpType
ACT = mybir.ActivationFunctionType
AXIS = mybir.AxisListType


def conditioned_residual_kernel(nc, x, itok_t, itok_e, T, Wi0, Wi1, Wo, sWi0, sWi1, sWo, g0, g1, out):
    P = 128
    B, S, D = x.shape
    F = sWi0.shape[1]
    K_STEPS, N_EXPERTS = T.shape[0], Wi0.shape[0]
    DC, SC, FC = D // P, S // P, F // P
    HALF = F // 2
    FPH = FC // 2
    FPT = 2
    TPN = FC // FPT
    TILES = 2 * TPN
    SHARED, EXPERT = 0, 1
    HI, LO = 0, 1
    PASSES = ((HI, HI), (HI, LO), (LO, HI))
    PIECES = 6
    G0_TILES = (6, 7)
    FILL = (3, 2, 3)
    WI_HALF0, WI_HALF1, WO = (0, 1), (2, 3), (4, 5)

    with ExitStack() as ctx:
        def sb(name, shape, dt=FP32):
            return ctx.enter_context(nc.sbuf_tensor(name, shape, dt))

        def ps(name, shape):
            return ctx.enter_context(nc.psum_tensor(name, shape, FP32))

        def sem(name):
            return ctx.enter_context(nc.semaphore(name))

        steps_sb = sb("steps_sb", [1, B], INT32)
        labels_sb = sb("labels_sb", [1, B], INT32)
        ident = sb("ident", [P, P])
        ones = sb("ones", [P, 1])
        act_warm = sb("act_warm", [P, 1])
        g0_sb = sb("g0_sb", [P, 2 * DC, D])
        g1_sb = sb("g1_sb", [P, DC, 2])
        raw = [sb(f"raw{k}", [P, 1024]) for k in range(PIECES)]
        wi_split = [sb(f"wi{m}_split", [P, 2, 2, DC, F], FP32R) for m in range(2)]
        wo_split = sb("wo_split", [P, 2, 2, FC, D], FP32R)
        T_sb = sb("T_sb", [P, SC, S])
        x_sb = sb("x_sb", [P, SC, D])
        x_split = sb("x_split", [P, 2, SC, D], FP32R)
        tT_split = sb("tT_split", [P, 2, SC, S], FP32R)
        h_sb = sb("h_sb", [P, SC, D])
        h_keep = sb("h_keep", [P, SC, D])
        hT_split = sb("hT_split", [P, 2, DC, S], FP32R)
        prod = sb("prod", [P, 2, FPT, S])
        prod_split = sb("prod_split", [P, 2, 2, FC, S], FP32R)
        g0T_sb = sb("g0T_sb", [P, DC, 2 * D])
        gate_row = sb("gate_row", [1, 2 * D])
        gate_in = sb("gate_in", [P, 2 * D])
        z_terms = sb("z_terms", [P, DC, 2 * D])
        z = sb("z", [P, DC])
        z_relu = sb("z_relu", [P, DC])
        l_part = sb("l_part", [P, 2])
        l_terms = sb("l_terms", [P, 2])
        logits = sb("logits", [P, 2])
        lmax = sb("lmax", [P, 1])
        lshift = sb("lshift", [P, 2])
        lexp = sb("lexp", [P, 2])
        lsum = sb("lsum", [P, 1])
        lrec = sb("lrec", [P, 1])
        wgt = sb("wgt", [P, 2])
        part = sb("part", [P, SC, D])
        out_sb = sb("out_sb", [P, SC, D])

        up_gate = [ps(f"up_gate{i}", [P, FPT, S]) for i in range(2)]
        up_lin = [ps(f"up_lin{i}", [P, FPT, S]) for i in range(2)]
        down = [ps(f"down{c}", [P, 2, D]) for c in range(SC)]
        front = ps("front", [P, 2, 256])
        g0T = ps("g0T", [P, 2 * D])

        steps_landed, labels_landed = sem("steps_landed"), sem("labels_landed")
        T_landed, x_landed = sem("T_landed"), sem("x_landed")
        g0_landed, g1_landed = sem("g0_landed"), sem("g1_landed")
        raw_landed = [sem(f"raw{k}_landed") for k in range(PIECES)]
        hi_done = [sem(f"hi{k}_done") for k in range(PIECES)]
        piece_split = [sem(f"piece{k}_split") for k in range(PIECES)]
        gelu_warm_done, exp_warm_done = sem("gelu_warm_done"), sem("exp_warm_done")
        ones_made, ident_made, ident_zeroed = sem("ones_made"), sem("ident_made"), sem("ident_zeroed")
        tT_ready, x_hi_done, tT_hi_done = sem("tT_ready"), sem("x_hi_done"), sem("tT_hi_done")
        x_lo_done, tT_lo_done = sem("x_lo_done"), sem("tT_lo_done")
        h_ready, h_done, h_kept = sem("h_ready"), sem("h_done"), sem("h_kept")
        hT_ready, hT_hi_done, hT_lo_done = sem("hT_ready"), sem("hT_hi_done"), sem("hT_lo_done")
        gate_ready, lin_ready = sem("gate_ready"), sem("lin_ready")
        gelu_done, prod_done = sem("gelu_done"), sem("prod_done")
        prod_hi_done, prod_lo_done = sem("prod_hi_done"), sem("prod_lo_done")
        down_ready = [sem(f"down{c}_ready") for c in range(SC)]
        g0T_ready, g0T_done = sem("g0T_ready"), sem("g0T_done")
        row_done, gate_in_ready = sem("row_done"), sem("gate_in_ready")
        z_done, z_relu_done, l_part_done = sem("z_done"), sem("z_relu_done"), sem("l_part_done")
        l_terms_done, logits_ready = sem("l_terms_done"), sem("logits_ready")
        max_done, shift_done, exp_done = sem("max_done"), sem("shift_done"), sem("exp_done")
        rec_done, wgt_done, part_done = sem("rec_done"), sem("wgt_done"), sem("part_done")
        final_done = [sem(f"final{c}_done") for c in range(SC)]
        out_stored = [sem(f"out{c}_stored") for c in range(SC)]

        def wait(eng, semaphore, value):
            if not isinstance(value, int) or value > 0:
                eng.wait_ge(semaphore, value)

        def piece_dst(n_is_shared, k, part_):
            net = SHARED if n_is_shared else EXPERT
            if k in WO:
                c = (k - WO[0]) * FPH
                return wo_split[:, net, part_, c:c + FPH, :]
            return wi_split[k % 2][:, net, part_, :, (k // 2) * HALF:(k // 2 + 1) * HALF]

        def raw_view(k):
            a = FPH if k in WO else DC
            return raw[k][:, :].rearrange("p (a n) -> p a n", a=a)

        def pieces_before(kind, b):
            if kind == "first":
                return {0: [(0, 2)], 1: [(0, 3)], 2: [(1, 0)], 3: [(1, 1)], 4: [(1, 2), (0, 4)], 5: [(1, 3)],
                        6: [(0, 5)], 7: [(1, 4)], TILES: [(1, 5)]}
            return {t: [(b + 1, k)] for t, k in ((0, 0), (1, 1), (2, 2), (3, 3), (4, 4), (6, 5))}

        def is_shared(n):
            return isinstance(n, int) and n == 0

        def over_batches(eng, body):
            body("first", 0)
            with eng.Fori(1, B - 1) as b:
                body("middle", b)
            body("last", B - 1)

        block = ctx.enter_context(nc.Block())

        @block.sync
        def _(sp):
            sp.dma_start(steps_sb[:, :], itok_t.rearrange("(o b) -> o b", o=1)).then_inc(steps_landed, 16)
            sp.dma_start(labels_sb[:, :], itok_e.rearrange("(o b) -> o b", o=1)).then_inc(labels_landed, 16)

            def load_x(b):
                wait(sp, h_done, b)
                sp.dma_start(x_sb[:, :, :], x[bass.ds(b, 1), :, :].rearrange("o (c p) d -> p (o c) d", p=P)
                             ).then_inc(x_landed, 16)

            def load_T(b):
                wait(sp, tT_ready, b)
                step = sp.value_load(steps_sb[0:1, bass.ds(b, 1)], min_val=1, max_val=K_STEPS)
                sp.dma_start(T_sb[:, :, :], T[bass.ds(step - 1, 1), :, :].rearrange("o (c p) s -> p (o c) s", p=P)
                             ).then_inc(T_landed, 16)

            def load_piece(n, k, label=None):
                wait(sp, piece_split[k], n)
                if is_shared(n):
                    src = (sWi0, sWi1)[k % 2] if k not in WO else sWo
                else:
                    w = (Wi0, Wi1)[k % 2] if k not in WO else Wo
                    src = w[bass.ds(label, 1), :, :].rearrange("o r c -> (o r) c")
                if k in WO:
                    h = k - WO[0]
                    src = src[h * HALF:(h + 1) * HALF, :].rearrange("(c p) n -> p c n", p=P)
                else:
                    h = k // 2
                    src = src[:, h * HALF:(h + 1) * HALF].rearrange("(c p) n -> p c n", p=P)
                sp.dma_start(raw_view(k), src).then_inc(raw_landed[k], 16)

            def expert_of(b):
                return sp.value_load(labels_sb[0:1, bass.ds(b, 1)], min_val=0, max_val=N_EXPERTS - 1)

            load_x(0)
            sp.wait_ge(steps_landed, 16)
            load_T(0)
            for k in range(PIECES):
                load_piece(0, k)
            sp.wait_ge(labels_landed, 16)
            label = expert_of(0)
            for k in WI_HALF0 + WI_HALF1:
                load_piece(1, k, label)
            load_x(1)
            load_T(1)
            sp.dma_start(g0_sb[:, :, :], g0.rearrange("(c p) n -> p c n", p=P)).then_inc(g0_landed, 16)
            sp.dma_start(g1_sb[:, :, :], g1.rearrange("(c p) n -> p c n", p=P)).then_inc(g1_landed, 16)
            for k in WO:
                load_piece(1, k, label)

            def load_expert(b):
                label = expert_of(b)
                for k in range(PIECES):
                    load_piece(b + 1, k, label)

            def store(b):
                for c in range(SC):
                    sp.wait_ge(final_done[c], b + 1)
                    sp.dma_start(out[bass.ds(b, 1), c * P:(c + 1) * P, :].rearrange("o p d -> p (o d)"),
                                 out_sb[:, c, :]).then_inc(out_stored[c], 16)

            with sp.Fori(0, B - 2) as b:
                load_expert(b + 1)
                load_T(b + 2)
                load_x(b + 2)
                store(b)
            load_expert(B - 1)
            store(B - 2)
            store(B - 1)
            for c in range(SC):
                sp.wait_ge(out_stored[c], 16 * B)

        @block.gpsimd
        def _(pool):
            nc.gpsimd.memset(ones[:, :], 1.0).then_inc(ones_made, 1)
            nc.gpsimd.memset(ident[:, :], 0.0).then_inc(ident_zeroed, 1)
            pool.wait_ge(ident_zeroed, 1)
            nc.gpsimd.affine_select(out=ident[:, :], in_=ident[:, :], compare_op=ALU.not_equal, fill=1.0, base=0,
                                    pattern=[[-1, P]], channel_multiplier=1).then_inc(ident_made, 1)

            for b in range(B):
                pool.wait_ge(row_done, b + 1)
                nc.gpsimd.partition_broadcast(gate_in[:, :], gate_row[0:1, :], P).then_inc(gate_in_ready, 1)
                pool.wait_ge(l_terms_done, b + 1)
                nc.gpsimd.partition_all_reduce(logits[:, :], l_terms[:, :], P, bass.bass_isa.ReduceOp.add
                                               ).then_inc(logits_ready, 1)

        @block.scalar
        def _(act):
            def x_hi(b):
                act.wait_ge(x_landed, 16 * (b + 1))
                wait(act, h_ready, b)
                nc.scalar.copy(x_split[:, HI], x_sb[:, :, :]).then_inc(x_hi_done, 1)

            def T_hi(b):
                act.wait_ge(tT_ready, b + 1)
                nc.scalar.copy(tT_split[:, HI], front[:, :, :]).then_inc(tT_hi_done, 1)

            def keep_h(b):
                act.wait_ge(h_done, b + 1)
                wait(act, final_done[SC - 1], b)
                nc.scalar.copy(h_keep[:, :, :], h_sb[:, :, :]).then_inc(h_kept, 1)

            def hT_hi(b):
                act.wait_ge(hT_ready, b + 1)
                nc.scalar.copy(hT_split[:, HI], front[:, :, :]).then_inc(hT_hi_done, 1)

            def piece_hi(n, k):
                act.wait_ge(raw_landed[k], 16 * (n + 1))
                if k in WO:
                    wait(act, down_ready[SC - 1], n - 1)
                elif not isinstance(n, int) or n > 1:
                    act.wait_ge(lin_ready, TILES * (n - 2) + TPN + (k // 2 + 1) * TPN // 2)
                nc.scalar.copy(piece_dst(is_shared(n), k, HI), raw_view(k)).then_inc(hi_done[k], 1)

            def prod_hi(b, t):
                net, tt = divmod(t, TPN)
                act.wait_ge(prod_done, TILES * b + t + 1)
                nc.scalar.copy(prod_split[:, net, HI, tt * FPT:(tt + 1) * FPT, :], prod[:, t % 2]
                               ).then_inc(prod_hi_done, 1)

            def batch(kind, b):
                sets = pieces_before(kind, b)
                for t in range(TILES):
                    for n, k in sets.get(t, ()):
                        piece_hi(n, k)
                    act.wait_ge(gate_ready, TILES * b + t + 1)
                    wait(act, prod_lo_done, TILES * b + t - 1)
                    nc.scalar.activation(prod[:, t % 2], up_gate[t % 2][:, :, :], ACT.Gelu_apprx_tanh
                                         ).then_inc(gelu_done, 1)
                    if t > 0:
                        prod_hi(b, t - 1)
                    if t == 1:
                        keep_h(b)
                    if t == 5 and kind != "last":
                        x_hi(b + 1)
                        T_hi(b + 1)
                    if kind == "first" and t in G0_TILES:
                        act.wait_ge(g0T_ready, G0_TILES.index(t) + 1)
                        nc.scalar.copy(g0T_sb[:, G0_TILES.index(t), :], g0T[:, :]).then_inc(g0T_done, 1)
                prod_hi(b, TILES - 1)
                for n, k in sets.get(TILES, ()):
                    piece_hi(n, k)
                act.wait_ge(down_ready[0], b + 1)
                nc.scalar.copy(gate_row[0:1, :], down[0][0:1, :, :].rearrange("p a d -> p (a d)")
                               ).then_inc(row_done, 1)
                if kind != "last":
                    hT_hi(b + 1)
                wait(act, exp_warm_done, b)
                nc.scalar.activation(act_warm[:, :], ones[:, :], ACT.Exp).then_inc(exp_warm_done, 1)
                act.wait_ge(shift_done, b + 1)
                nc.scalar.activation(lexp[:, :], lshift[:, :], ACT.Exp, accum_out=lsum[:, :]).then_inc(exp_done, 1)

            act.wait_ge(ones_made, 1)
            nc.scalar.activation(act_warm[:, :], ones[:, :], ACT.Gelu_apprx_tanh).then_inc(gelu_warm_done, 1)
            act.wait_ge(gelu_warm_done, 1)
            x_hi(0)
            T_hi(0)
            piece_hi(0, 0)
            piece_hi(0, 1)
            hT_hi(0)
            over_batches(act, batch)

        @block.vector
        def _(dve):
            def f32(ap):
                return ap.bitcast(FP32)

            def x_and_T_lo(b):
                dve.wait_ge(x_hi_done, b + 1)
                nc.vector.tensor_tensor(x_split[:, LO], x_sb[:, :, :], f32(x_split[:, HI]), ALU.subtract
                                        ).then_inc(x_lo_done, 1)
                dve.wait_ge(tT_hi_done, b + 1)
                nc.vector.tensor_tensor(tT_split[:, LO], front[:, :, :], f32(tT_split[:, HI]), ALU.subtract
                                        ).then_inc(tT_lo_done, 1)

            def h_add(b):
                dve.wait_ge(h_ready, b + 1)
                wait(dve, h_kept, b)
                nc.vector.tensor_tensor(h_sb[:, :, :], front[:, :, :], x_sb[:, :, :], ALU.add).then_inc(h_done, 1)

            def hT_lo(b):
                dve.wait_ge(hT_hi_done, b + 1)
                nc.vector.tensor_tensor(hT_split[:, LO], front[:, :, :], f32(hT_split[:, HI]), ALU.subtract
                                        ).then_inc(hT_lo_done, 1)

            def piece_lo(n, k):
                dve.wait_ge(hi_done[k], n + 1)
                nc.vector.tensor_tensor(piece_dst(is_shared(n), k, LO), raw_view(k),
                                        f32(piece_dst(is_shared(n), k, HI)), ALU.subtract).then_inc(piece_split[k], 1)

            def prod_lo(b, t):
                net, tt = divmod(t, TPN)
                fs = slice(tt * FPT, (tt + 1) * FPT)
                dve.wait_ge(prod_hi_done, TILES * b + t + 1)
                nc.vector.tensor_tensor(prod_split[:, net, LO, fs, :], prod[:, t % 2],
                                        f32(prod_split[:, net, HI, fs, :]), ALU.subtract).then_inc(prod_lo_done, 1)

            def batch(kind, b):
                sets = pieces_before(kind, b)
                for t in range(TILES):
                    for n, k in sets.get(t, ()):
                        piece_lo(n, k)
                    dve.wait_ge(gelu_done, TILES * b + t + 1)
                    dve.wait_ge(lin_ready, TILES * b + t + 1)
                    nc.vector.tensor_tensor(prod[:, t % 2], up_lin[t % 2][:, :, :], prod[:, t % 2], ALU.mult
                                            ).then_inc(prod_done, 1)
                    if t > 0:
                        prod_lo(b, t - 1)
                    if t == 5 and kind != "last":
                        x_and_T_lo(b + 1)
                prod_lo(b, TILES - 1)
                if kind != "last":
                    h_add(b + 1)
                for n, k in sets.get(TILES, ()):
                    piece_lo(n, k)
                if kind != "last":
                    hT_lo(b + 1)
                if kind == "first":
                    dve.wait_ge(g0T_done, DC)
                    dve.wait_ge(g1_landed, 16)
                dve.wait_ge(gate_in_ready, b + 1)
                for m in range(DC):
                    nc.vector.scalar_tensor_tensor(out=z_terms[:, m, :], in0=gate_in[:, :], scalar=1.0,
                                                   in1=g0T_sb[:, m, :], op0=ALU.mult, op1=ALU.mult,
                                                   accum_out=z[:, m:m + 1]).then_inc(z_done, 1)
                dve.wait_ge(z_done, DC * (b + 1))
                nc.vector.tensor_scalar_max(z_relu[:, :], z[:, :], 0.0).then_inc(z_relu_done, 1)
                dve.wait_ge(z_relu_done, b + 1)
                nc.vector.tensor_scalar(l_part[:, :], g1_sb[:, 0, :], z_relu[:, 0:1], None, ALU.mult
                                        ).then_inc(l_part_done, 1)
                dve.wait_ge(l_part_done, b + 1)
                nc.vector.scalar_tensor_tensor(out=l_terms[:, :], in0=g1_sb[:, 1, :], scalar=z_relu[:, 1:2],
                                               in1=l_part[:, :], op0=ALU.mult, op1=ALU.add
                                               ).then_inc(l_terms_done, 1)
                dve.wait_ge(logits_ready, b + 1)
                nc.vector.reduce_max(lmax[:, :], logits[:, :], AXIS.X).then_inc(max_done, 1)
                dve.wait_ge(max_done, b + 1)
                nc.vector.tensor_scalar(lshift[:, :], logits[:, :], lmax[:, :], None, ALU.subtract).then_inc(shift_done, 1)
                dve.wait_ge(exp_done, b + 1)
                nc.vector.reciprocal(lrec[:, :], lsum[:, :]).then_inc(rec_done, 1)
                dve.wait_ge(rec_done, b + 1)
                nc.vector.tensor_scalar(wgt[:, :], lexp[:, :], lrec[:, :], None, ALU.mult).then_inc(wgt_done, 1)
                dve.wait_ge(wgt_done, b + 1)
                dve.wait_ge(h_kept, b + 1)
                for c in range(SC):
                    dve.wait_ge(down_ready[c], b + 1)
                    wait(dve, out_stored[c], 16 * b)
                    nc.vector.scalar_tensor_tensor(out=part[:, c, :], in0=down[c][:, 0, :], scalar=wgt[:, 0:1],
                                                   in1=h_keep[:, c, :], op0=ALU.mult, op1=ALU.add
                                                   ).then_inc(part_done, 1)
                    dve.wait_ge(part_done, SC * b + c + 1)
                    nc.vector.scalar_tensor_tensor(out=out_sb[:, c, :], in0=down[c][:, 1, :], scalar=wgt[:, 1:2],
                                                   in1=part[:, c, :], op0=ALU.mult, op1=ALU.add
                                                   ).then_inc(final_done[c], 1)

            x_and_T_lo(0)
            piece_lo(0, 0)
            h_add(0)
            piece_lo(0, 1)
            hT_lo(0)
            over_batches(dve, batch)

        @block.tensor
        def _(pe):
            def transposes(src):
                for r in range(2):
                    for c in range(2):
                        last = nc.tensor.transpose(front[:, c, r * P:(r + 1) * P], src[:, r, c * P:(c + 1) * P],
                                                   ident[:, :])
                return last

            def T_transposed(b):
                pe.wait_ge(T_landed, 16 * (b + 1))
                wait(pe, hT_lo_done, b)
                transposes(T_sb).then_inc(tT_ready, 1)

            def h_product(b):
                pe.wait_ge(x_lo_done, b + 1)
                pe.wait_ge(tT_lo_done, b + 1)
                for c in range(SC):
                    terms = [(j, l, r) for j in range(SC) for l, r in PASSES]
                    for i, (j, l, r) in enumerate(terms):
                        last = nc.tensor.matmul(front[:, c, :], tT_split[:, l, j, c * P:(c + 1) * P],
                                                x_split[:, r, j, :], start=i == 0, stop=i == len(terms) - 1)
                last.then_inc(h_ready, 1)

            def h_transposed(b):
                pe.wait_ge(h_done, b + 1)
                transposes(h_sb).then_inc(hT_ready, 1)

            def up_tile(b, t):
                net, tt = divmod(t, TPN)
                wait(pe, prod_done, TILES * b + t - 1)
                for m, (bank, ready) in enumerate(((up_gate[t % 2], gate_ready), (up_lin[t % 2], lin_ready))):
                    for j in range(FPT):
                        f = tt * FPT + j
                        terms = [(c, l, r) for c in range(DC) for l, r in PASSES]
                        for i, (c, l, r) in enumerate(terms):
                            last = nc.tensor.matmul(bank[:, j, :], wi_split[m][:, net, l, c, f * P:(f + 1) * P],
                                                    hT_split[:, r, c, :], start=i == 0, stop=i == len(terms) - 1)
                    last.then_inc(ready, 1)

            def down_chunk(c, net):
                col = {EXPERT: 0, SHARED: 1}[net]
                terms = [(f, l, r) for f in range(FC) for l, r in PASSES]
                for i, (f, l, r) in enumerate(terms):
                    last = nc.tensor.matmul(down[c][:, col, :], prod_split[:, net, l, f, c * P:(c + 1) * P],
                                            wo_split[:, net, r, f, :], start=i == 0, stop=i == len(terms) - 1)
                return last

            def batch(kind, b):
                pe.wait_ge(hT_lo_done, b + 1)
                for t in range(TILES):
                    net = t // TPN
                    if t % TPN in (0, TPN // 2):
                        half = (t % TPN) // (TPN // 2)
                        for k in (WI_HALF0, WI_HALF1)[half]:
                            if net == EXPERT:
                                pe.wait_ge(piece_split[k], b + 2)
                            elif kind == "first":
                                pe.wait_ge(piece_split[k], 1)
                    up_tile(b, t)
                    if t == 5 and kind != "last":
                        T_transposed(b + 1)
                    if kind == "first" and t in G0_TILES:
                        m = G0_TILES.index(t)
                        pe.wait_ge(g0_landed, 16)
                        wait(pe, g0T_done, m)
                        for c in range(2 * DC):
                            last = nc.tensor.transpose(g0T[:, c * P:(c + 1) * P],
                                                       g0_sb[:, c, m * P:(m + 1) * P], ident[:, :])
                        last.then_inc(g0T_ready, 1)
                if kind != "last":
                    h_product(b + 1)
                if kind == "first":
                    for k in WO:
                        pe.wait_ge(piece_split[k], 1)
                pe.wait_ge(prod_lo_done, TILES * b + TPN)
                wait(pe, final_done[0], b)
                down_chunk(0, SHARED)
                pe.wait_ge(prod_lo_done, TILES * (b + 1))
                for k in WO:
                    pe.wait_ge(piece_split[k], b + 2)
                down_chunk(0, EXPERT).then_inc(down_ready[0], 1)
                if kind != "last":
                    h_transposed(b + 1)
                wait(pe, final_done[1], b)
                down_chunk(1, SHARED)
                down_chunk(1, EXPERT).then_inc(down_ready[1], 1)

            def stay_warm(n):
                for _ in range(n):
                    nc.tensor.matmul(up_lin[1][:, 0, 0:P], ident[:, :], ident[:, :], start=True, stop=True)

            pe.wait_ge(ident_made, 1)
            stay_warm(10)
            T_transposed(0)
            stay_warm(FILL[0])
            h_product(0)
            stay_warm(FILL[1])
            h_transposed(0)
            stay_warm(FILL[2])
            over_batches(pe, batch)


_INS = ['x', 'itok_B_1_98', 'itok_B_0_2', 'L0_cond_T', 'L1_cond_Wi0', 'L1_cond_Wi1', 'L1_cond_Wo',
        'L1_cond_sWi0', 'L1_cond_sWi1', 'L1_cond_sWo', 'L1_cond_g0', 'L1_cond_g1']


def kernel(**inputs):
    import numpy as _np
    import concourse.bacc as _bacc
    from concourse import mybir as _mybir
    from concourse.bass_utils import run_bass_kernel_spmd as _run

    nc = _bacc.Bacc("TRN2", target_bir_lowering=False, num_devices=1)
    arrays, args = {}, []
    for name in _INS:
        a = _np.ascontiguousarray(inputs[name])
        arrays[f"in_{name}_dram"] = a
        args.append(nc.dram_tensor(f"in_{name}_dram", a.shape, _mybir.dt.from_np(a.dtype), kind="ExternalInput").ap())
    out = nc.dram_tensor("out_0_dram", inputs['x'].shape, _mybir.dt.float32, kind="ExternalOutput").ap()
    conditioned_residual_kernel(nc, *args, out)
    r = _run(nc, [arrays], core_ids=[0])
    return r.results[0]["out_0_dram"]
```

```python
import concourse.bass as bass
from concourse import mybir
from contextlib import ExitStack

FP32 = mybir.dt.float32
FP32R = mybir.dt.float32r
INT32 = mybir.dt.int32
ALU = mybir.AluOpType
ACT = mybir.ActivationFunctionType
AXIS = mybir.AxisListType


def conditioned_residual_kernel(nc, x, itok_t, itok_e, T, Wi0, Wi1, Wo, sWi0, sWi1, sWo, g0, g1, out):
    P = 128
    B, S, D = x.shape
    F = sWi0.shape[1]
    K_STEPS, N_EXPERTS = T.shape[0], Wi0.shape[0]
    DC, SC, FC = D // P, S // P, F // P
    HALF = F // 2
    FPH = FC // 2
    FPT = 2
    TPN = FC // FPT
    HALF_TILES = TPN // 2
    TILES = 2 * TPN
    SHARED, EXPERT = 0, 1
    HI, LO = 0, 1
    PASSES = ((HI, HI), (HI, LO), (LO, HI))
    PIECES = 6
    WI_HALF0, WI_HALF1, WO = (0, 1), (2, 3), (4, 5)
    POOL_PIECES = ((0, 4), (0, 5), (1, 4), (1, 5))
    BLK = 32
    Q = P // BLK
    TURN_T, SPLIT_T = {"first": 0, "middle": 2}, {"first": 2, "middle": 4}
    H_TILE = 6
    FILL = (10, 2, 2)

    h_spill = nc.dram_tensor("h_spill", (Q, Q, BLK, DC * SC * BLK), FP32, kind="Internal").ap()

    with ExitStack() as ctx:
        def sb(name, shape, dt=FP32):
            return ctx.enter_context(nc.sbuf_tensor(name, shape, dt))

        def ps(name, shape):
            return ctx.enter_context(nc.psum_tensor(name, shape, FP32))

        def sem(name):
            return ctx.enter_context(nc.semaphore(name))

        steps_sb = sb("steps_sb", [1, B], INT32)
        labels_sb = sb("labels_sb", [1, B], INT32)
        ident = sb("ident", [P, P])
        ones = sb("ones", [P, 1])
        act_warm = sb("act_warm", [P, 1])
        g0_sb = sb("g0_sb", [P, 2 * DC, D])
        g1_sb = sb("g1_sb", [P, DC, 2])
        raw = [sb(f"raw{k}", [P, 1024]) for k in range(PIECES)]
        wi_split = [sb(f"wi{m}_split", [P, 2, 2, DC, F], FP32R) for m in range(2)]
        wo_split = sb("wo_split", [P, 2, 2, FC, D], FP32R)
        T_sb = sb("T_sb", [P, SC, S])
        T_blocks = sb("T_blocks", [P, SC, SC, Q, BLK])
        x_sb = sb("x_sb", [P, SC, D])
        x_split = sb("x_split", [P, 2, SC, D], FP32R)
        tT_split = sb("tT_split", [P, 2, SC, S], FP32R)
        h_sb = sb("h_sb", [P, SC, D])
        h_keep = sb("h_keep", [P, SC, D])
        tT_sb = sb("tT_sb", [P, SC, S])
        h_blocks = sb("h_blocks", [P, Q, DC, SC, BLK])
        hT_blocks = sb("hT_blocks", [P, Q, DC, SC, BLK])
        hT_split = sb("hT_split", [P, 2, DC, S], FP32R)
        prod = sb("prod", [P, 2, FPT, S])
        prod_split = sb("prod_split", [P, 2, 2, FC, S], FP32R)
        g0T_sb = sb("g0T_sb", [P, DC, 2 * D])
        gate_row = sb("gate_row", [1, 2 * D])
        gate_in = sb("gate_in", [P, 2 * D])
        z_terms = sb("z_terms", [P, DC, 2 * D])
        z = sb("z", [P, DC])
        z_relu = sb("z_relu", [P, DC])
        l_part = sb("l_part", [P, 2])
        l_terms = sb("l_terms", [P, 2])
        logits = sb("logits", [P, 2])
        lmax = sb("lmax", [P, 1])
        lshift = sb("lshift", [P, 2])
        lexp = sb("lexp", [P, 2])
        lsum = sb("lsum", [P, 1])
        lrec = sb("lrec", [P, 1])
        wgt = sb("wgt", [P, 2])
        part = sb("part", [P, SC, D])
        out_sb = sb("out_sb", [P, SC, D])

        up_gate = [ps(f"up_gate{i}", [P, FPT, S]) for i in range(2)]
        up_lin = [ps(f"up_lin{i}", [P, FPT, S]) for i in range(2)]
        down = [ps(f"down{c}", [P, 2, D]) for c in range(SC)]
        front = ps("front", [P, SC, D])
        spare = ps("spare", [P, SC, D])
        turned0, h_rows0, g0T = (front, spare), down, down

        steps_landed, labels_landed = sem("steps_landed"), sem("labels_landed")
        T_landed, x_landed = sem("T_landed"), sem("x_landed")
        g0_landed, g1_landed = sem("g0_landed"), sem("g1_landed")
        raw_landed = [sem(f"raw{k}_landed") for k in range(PIECES)]
        hi_done = [sem(f"hi{k}_done") for k in range(PIECES)]
        piece_split = [sem(f"piece{k}_split") for k in range(PIECES)]
        gelu_warm_done, exp_warm_done = sem("gelu_warm_done"), sem("exp_warm_done")
        ones_made, ident_made, ident_zeroed = sem("ones_made"), sem("ident_made"), sem("ident_zeroed")
        tT_ready, x_hi_done, tT_hi_done = sem("tT_ready"), sem("x_hi_done"), sem("tT_hi_done")
        T_blocks_landed, T_turned = sem("T_blocks_landed"), sem("T_turned")
        h_turned, h_spilled, hT_landed = sem("h_turned"), sem("h_spilled"), sem("hT_landed")
        x_lo_done, tT_lo_done = sem("x_lo_done"), sem("tT_lo_done")
        h_ready, h_done, h_kept = sem("h_ready"), sem("h_done"), sem("h_kept")
        hT_ready, hT_hi_done, hT_lo_done = sem("hT_ready"), sem("hT_hi_done"), sem("hT_lo_done")
        gate_ready, lin_ready = sem("gate_ready"), sem("lin_ready")
        gelu_done, prod_done = sem("gelu_done"), sem("prod_done")
        prod_hi_done, prod_lo_done = sem("prod_hi_done"), sem("prod_lo_done")
        down_ready = [sem(f"down{c}_ready") for c in range(SC)]
        g0T_ready, g0T_done = sem("g0T_ready"), sem("g0T_done")
        half = {s: sem(f"half_{name}") for name, s in (
            ("T_landed", T_landed), ("tT_ready", tT_ready), ("tT_hi_done", tT_hi_done), ("tT_lo_done", tT_lo_done),
            ("h_ready", h_ready), ("h_done", h_done), ("hT_ready", hT_ready), ("hT_hi_done", hT_hi_done),
            ("hT_lo_done", hT_lo_done))}
        row_done, gate_in_ready = sem("row_done"), sem("gate_in_ready")
        z_done, z_relu_done, l_part_done = sem("z_done"), sem("z_relu_done"), sem("l_part_done")
        l_terms_done, logits_ready = sem("l_terms_done"), sem("logits_ready")
        max_done, shift_done, exp_done = sem("max_done"), sem("shift_done"), sem("exp_done")
        rec_done, wgt_done, part_done = sem("rec_done"), sem("wgt_done"), sem("part_done")
        final_done = [sem(f"final{c}_done") for c in range(SC)]
        out_stored = [sem(f"out{c}_stored") for c in range(SC)]

        def of_half(r, semaphore):
            return half[semaphore] if r == 0 else semaphore

        def wait(eng, semaphore, value):
            if not isinstance(value, int) or value > 0:
                eng.wait_ge(semaphore, value)

        def piece_dst(n_is_shared, k, part_):
            net = SHARED if n_is_shared else EXPERT
            if k in WO:
                c = (k - WO[0]) * FPH
                return wo_split[:, net, part_, c:c + FPH, :]
            return wi_split[k % 2][:, net, part_, :, (k // 2) * HALF:(k // 2 + 1) * HALF]

        def raw_view(k):
            a = FPH if k in WO else DC
            return raw[k][:, :].rearrange("p (a n) -> p a n", a=a)

        def pieces_before(kind, b):
            if kind == "first":
                return {0: [(0, 2), (0, 3)], 2: [(1, 0)], 3: [(1, 1), (0, 4)], 4: [(1, 2), (0, 5)], 5: [(1, 3)],
                        6: [(1, 4)], 7: [(1, 5)]}
            return {t: [(b + 1, k)] for t, k in ((0, 0), (1, 1), (2, 2), (3, 3), (4, 4), (6, 5))}

        def is_first(n):
            return isinstance(n, int) and n == 0

        is_shared = is_first

        def turned_h():
            return hT_blocks[:, :, :, :, :].rearrange("p q c s r -> p (c s) q r")

        def hT_in_order(part_):
            return hT_split[:, part_].rearrange("p c (s q r) -> p (c s) q r", s=SC, q=Q)

        def rows0(split, part_, r):
            return split[:, part_, :, r * P:(r + 1) * P]

        def turned_rows0(r):
            return turned0[r][:, 0, :].rearrange("p (c k) -> p c k", c=DC)

        def over_batches(eng, body):
            body("first", 0)
            with eng.Fori(1, B - 1) as b:
                body("middle", b)
            body("last", B - 1)

        block = ctx.enter_context(nc.Block())

        @block.sync
        def _(sp):
            sp.dma_start(steps_sb[:, :], itok_t.rearrange("(o b) -> o b", o=1)).then_inc(steps_landed, 16)
            sp.dma_start(labels_sb[:, :], itok_e.rearrange("(o b) -> o b", o=1)).then_inc(labels_landed, 16)

            def load_x(b):
                wait(sp, h_done, b)
                sp.dma_start(x_sb[:, :, :], x[bass.ds(b, 1), :, :].rearrange("o (c p) d -> p (o c) d", p=P)
                             ).then_inc(x_landed, 16)

            def load_T(b):
                step = sp.value_load(steps_sb[0:1, bass.ds(b, 1)], min_val=1, max_val=K_STEPS)
                src = T[bass.ds(step - 1, 1), :, :]
                if is_first(b):
                    for r in range(SC):
                        sp.dma_start(T_sb[:, r], src[:, r * P:(r + 1) * P, :].rearrange("o p s -> p (o s)")
                                     ).then_inc(of_half(r, T_landed), 16)
                    return
                wait(sp, T_turned, b - 1)
                for q in range(Q):
                    for c in range(SC):
                        col = c * P + q * BLK
                        sp.dma_start(T_blocks[q * BLK:(q + 1) * BLK, c].rearrange("p a g k -> p (a g) k"),
                                     src[:, :, col:col + BLK].rearrange("o (a r) k -> r (o a) k", r=BLK)
                                     ).then_inc(T_blocks_landed, 16)

            def load_piece(n, k, label=None):
                wait(sp, piece_split[k], n)
                if is_shared(n):
                    src = (sWi0, sWi1)[k % 2] if k not in WO else sWo
                else:
                    w = (Wi0, Wi1)[k % 2] if k not in WO else Wo
                    src = w[bass.ds(label, 1), :, :].rearrange("o r c -> (o r) c")
                if k in WO:
                    h = k - WO[0]
                    src = src[h * HALF:(h + 1) * HALF, :].rearrange("(c p) n -> p c n", p=P)
                else:
                    h = k // 2
                    src = src[:, h * HALF:(h + 1) * HALF].rearrange("(c p) n -> p c n", p=P)
                sp.dma_start(raw_view(k), src).then_inc(raw_landed[k], 16)

            def swap_h_blocks(b):
                sp.wait_ge(h_turned, b)
                for q in range(Q):
                    sp.dma_start(h_spill[q].rearrange("g t n -> t g n"),
                                 h_blocks[q * BLK:(q + 1) * BLK].rearrange("t g c s r -> t g (c s r)")
                                 ).then_inc(h_spilled, 16)
                sp.wait_ge(h_spilled, 16 * Q * b)
                sp.wait_ge(hT_lo_done, b)
                sp.dma_start(hT_blocks[:, :].rearrange("p q c s r -> p q (c s r)"),
                             h_spill.rearrange("q g t n -> (g t) q n")).then_inc(hT_landed, 16)

            def expert_of(b):
                return sp.value_load(labels_sb[0:1, bass.ds(b, 1)], min_val=0, max_val=N_EXPERTS - 1)

            load_x(0)
            sp.wait_ge(steps_landed, 16)
            load_T(0)
            for k in WI_HALF0:
                load_piece(0, k)
            sp.dma_start(g0_sb[:, :, :], g0.rearrange("(c p) n -> p c n", p=P)).then_inc(g0_landed, 16)
            for k in WI_HALF1:
                load_piece(0, k)
            load_T(1)
            load_x(1)
            sp.wait_ge(labels_landed, 16)
            label = expert_of(0)
            for k in WI_HALF0:
                load_piece(1, k, label)
            for k in WO:
                load_piece(0, k)
            for k in WI_HALF1:
                load_piece(1, k, label)
            sp.dma_start(g1_sb[:, :, :], g1.rearrange("(c p) n -> p c n", p=P)).then_inc(g1_landed, 16)
            for k in WO:
                load_piece(1, k, label)

            def load_expert(b):
                label = expert_of(b)
                for k in range(PIECES):
                    load_piece(b + 1, k, label)
                    if k == 4:
                        swap_h_blocks(b)

            def store(b):
                for c in range(SC):
                    sp.wait_ge(final_done[c], b + 1)
                    sp.dma_start(out[bass.ds(b, 1), c * P:(c + 1) * P, :].rearrange("o p d -> p (o d)"),
                                 out_sb[:, c, :]).then_inc(out_stored[c], 16)

            with sp.Fori(0, B - 2) as b:
                load_expert(b + 1)
                load_T(b + 2)
                load_x(b + 2)
                store(b)
            load_expert(B - 1)
            store(B - 2)
            store(B - 1)
            for c in range(SC):
                sp.wait_ge(out_stored[c], 16 * B)

        @block.gpsimd
        def _(pool):
            nc.gpsimd.memset(ones[:, :], 1.0).then_inc(ones_made, 1)
            nc.gpsimd.memset(ident[:, :], 0.0).then_inc(ident_zeroed, 1)
            pool.wait_ge(ident_zeroed, 1)
            nc.gpsimd.affine_select(out=ident[:, :], in_=ident[:, :], compare_op=ALU.not_equal, fill=1.0, base=0,
                                    pattern=[[-1, P]], channel_multiplier=1).then_inc(ident_made, 1)

            for n, k in POOL_PIECES:
                pool.wait_ge(hi_done[k], n + 1)
                nc.gpsimd.tensor_tensor(piece_dst(is_shared(n), k, LO), raw_view(k),
                                        piece_dst(is_shared(n), k, HI).bitcast(FP32), ALU.subtract
                                        ).then_inc(piece_split[k], 1)

            for b in range(B):
                pool.wait_ge(row_done, b + 1)
                nc.gpsimd.partition_broadcast(gate_in[:, :], gate_row[0:1, :], P).then_inc(gate_in_ready, 1)
                pool.wait_ge(l_terms_done, b + 1)
                nc.gpsimd.partition_all_reduce(logits[:, :], l_terms[:, :], P, bass.bass_isa.ReduceOp.add
                                               ).then_inc(logits_ready, 1)

        @block.scalar
        def _(act):
            def x_hi(b):
                act.wait_ge(x_landed, 16 * (b + 1))
                wait(act, h_ready, b)
                nc.scalar.copy(x_split[:, HI], x_sb[:, :, :]).then_inc(x_hi_done, 1)

            def T_hi(b):
                act.wait_ge(T_turned, b)
                nc.scalar.copy(tT_split[:, HI], tT_sb[:, :, :]).then_inc(tT_hi_done, 1)

            def keep_h(b):
                act.wait_ge(h_done, b + 1)
                wait(act, final_done[SC - 1], b)
                nc.scalar.copy(h_keep[:, :, :], h_sb[:, :, :]).then_inc(h_kept, 1)

            def hT_hi(b):
                act.wait_ge(hT_landed, 16 * b)
                act.wait_ge(lin_ready, TILES * b)
                nc.scalar.copy(hT_in_order(HI), turned_h()).then_inc(hT_hi_done, 1)

            def piece_hi(n, k):
                act.wait_ge(raw_landed[k], 16 * (n + 1))
                if k in WO:
                    wait(act, down_ready[SC - 1], n - 1)
                elif not isinstance(n, int) or n > 1:
                    act.wait_ge(lin_ready, TILES * (n - 2) + TPN + (k // 2 + 1) * TPN // 2)
                nc.scalar.copy(piece_dst(is_shared(n), k, HI), raw_view(k)).then_inc(hi_done[k], 1)

            def prod_hi(b, t):
                net, tt = divmod(t, TPN)
                act.wait_ge(prod_done, TILES * b + t + 1)
                nc.scalar.copy(prod_split[:, net, HI, tt * FPT:(tt + 1) * FPT, :], prod[:, t % 2]
                               ).then_inc(prod_hi_done, 1)

            def batch(kind, b):
                sets = pieces_before(kind, b)
                for t in range(TILES):
                    for n, k in sets.get(t, ()):
                        piece_hi(n, k)
                    act.wait_ge(gate_ready, TILES * b + t + 1)
                    wait(act, prod_lo_done, TILES * b + t - 1)
                    nc.scalar.activation(prod[:, t % 2], up_gate[t % 2][:, :, :], ACT.Gelu_apprx_tanh
                                         ).then_inc(gelu_done, 1)
                    if t > 0:
                        prod_hi(b, t - 1)
                    if t == 1:
                        keep_h(b)
                    if t == SPLIT_T.get(kind):
                        x_hi(b + 1)
                        T_hi(b + 1)
                    if kind == "first" and t == 0:
                        for m in range(DC):
                            act.wait_ge(g0T_ready, m + 1)
                            nc.scalar.copy(g0T_sb[:, m, :], g0T[m][:, :, :].rearrange("p a d -> p (a d)")
                                           ).then_inc(g0T_done, 1)
                prod_hi(b, TILES - 1)
                act.wait_ge(down_ready[0], b + 1)
                nc.scalar.copy(gate_row[0:1, :], down[0][0:1, :, :].rearrange("p a d -> p (a d)")
                               ).then_inc(row_done, 1)
                if kind != "last":
                    hT_hi(b + 1)
                wait(act, exp_warm_done, b)
                nc.scalar.activation(act_warm[:, :], ones[:, :], ACT.Exp).then_inc(exp_warm_done, 1)
                act.wait_ge(shift_done, b + 1)
                nc.scalar.activation(lexp[:, :], lshift[:, :], ACT.Exp, accum_out=lsum[:, :]).then_inc(exp_done, 1)

            act.wait_ge(ones_made, 1)
            nc.scalar.activation(act_warm[:, :], ones[:, :], ACT.Gelu_apprx_tanh).then_inc(gelu_warm_done, 1)
            act.wait_ge(gelu_warm_done, 1)
            x_hi(0)
            for r in range(SC):
                act.wait_ge(of_half(r, tT_ready), 1)
                nc.scalar.copy(rows0(tT_split, HI, r), turned_rows0(r)).then_inc(of_half(r, tT_hi_done), 1)
            piece_hi(0, 0)
            for r in range(SC):
                act.wait_ge(of_half(r, hT_ready), 1)
                nc.scalar.copy(rows0(hT_split, HI, r), turned_rows0(r)).then_inc(of_half(r, hT_hi_done), 1)
            piece_hi(0, 1)
            over_batches(act, batch)

        @block.vector
        def _(dve):
            def f32(ap):
                return ap.bitcast(FP32)

            def x_lo(b):
                dve.wait_ge(x_hi_done, b + 1)
                nc.vector.tensor_tensor(x_split[:, LO], x_sb[:, :, :], f32(x_split[:, HI]), ALU.subtract
                                        ).then_inc(x_lo_done, 1)

            def T_lo(b):
                dve.wait_ge(tT_hi_done, b + 1)
                nc.vector.tensor_tensor(tT_split[:, LO], tT_sb[:, :, :], f32(tT_split[:, HI]), ALU.subtract
                                        ).then_inc(tT_lo_done, 1)

            def turn_T(b):
                dve.wait_ge(T_blocks_landed, 16 * Q * SC * b)
                wait(dve, tT_lo_done, b)
                nc.vector.transpose(tT_sb[:, :, :].bitcast(INT32).rearrange("p c (a r) -> p (c a) r", r=BLK),
                                    T_blocks[:, :, :, :, :].bitcast(INT32).rearrange("p c a g k -> p (c a g) k")
                                    ).then_inc(T_turned, 1)

            def turn_h(b):
                dve.wait_ge(h_done, b + 1)
                wait(dve, hT_landed, 16 * (b - 1))
                for c in range(SC):
                    last = nc.vector.transpose(
                        h_blocks[:, :, :, c, :].bitcast(INT32).rearrange("p g c r -> p c g r"),
                        h_sb[:, c, :].bitcast(INT32).rearrange("p (c g r) -> p c g r", c=DC, g=Q))
                last.then_inc(h_turned, 1)

            def h_add(b):
                dve.wait_ge(h_ready, b + 1)
                wait(dve, h_kept, b)
                nc.vector.tensor_tensor(h_sb[:, :, :], front[:, :, :], x_sb[:, :, :], ALU.add).then_inc(h_done, 1)

            def hT_lo(b):
                dve.wait_ge(hT_hi_done, b + 1)
                nc.vector.tensor_tensor(hT_in_order(LO), turned_h(), f32(hT_in_order(HI)),
                                        ALU.subtract).then_inc(hT_lo_done, 1)

            def piece_lo(n, k):
                if isinstance(n, int) and (n, k) in POOL_PIECES:
                    return
                dve.wait_ge(hi_done[k], n + 1)
                nc.vector.tensor_tensor(piece_dst(is_shared(n), k, LO), raw_view(k),
                                        f32(piece_dst(is_shared(n), k, HI)), ALU.subtract).then_inc(piece_split[k], 1)

            def prod_lo(b, t):
                net, tt = divmod(t, TPN)
                fs = slice(tt * FPT, (tt + 1) * FPT)
                dve.wait_ge(prod_hi_done, TILES * b + t + 1)
                nc.vector.tensor_tensor(prod_split[:, net, LO, fs, :], prod[:, t % 2],
                                        f32(prod_split[:, net, HI, fs, :]), ALU.subtract).then_inc(prod_lo_done, 1)

            def batch(kind, b):
                sets = pieces_before(kind, b)
                for t in range(TILES):
                    for n, k in sets.get(t, ()):
                        piece_lo(n, k)
                    if t == H_TILE + 1 and kind != "last":
                        h_add(b + 1)
                        turn_h(b + 1)
                    dve.wait_ge(gelu_done, TILES * b + t + 1)
                    dve.wait_ge(lin_ready, TILES * b + t + 1)
                    nc.vector.tensor_tensor(prod[:, t % 2], up_lin[t % 2][:, :, :], prod[:, t % 2], ALU.mult
                                            ).then_inc(prod_done, 1)
                    if t > 0:
                        prod_lo(b, t - 1)
                    if t == TURN_T.get(kind):
                        turn_T(b + 1)
                    if t == SPLIT_T.get(kind):
                        x_lo(b + 1)
                        T_lo(b + 1)
                prod_lo(b, TILES - 1)
                if kind == "first":
                    dve.wait_ge(g0T_done, DC)
                    dve.wait_ge(g1_landed, 16)
                dve.wait_ge(gate_in_ready, b + 1)
                for m in range(DC):
                    nc.vector.scalar_tensor_tensor(out=z_terms[:, m, :], in0=gate_in[:, :], scalar=1.0,
                                                   in1=g0T_sb[:, m, :], op0=ALU.mult, op1=ALU.mult,
                                                   accum_out=z[:, m:m + 1]).then_inc(z_done, 1)
                dve.wait_ge(z_done, DC * (b + 1))
                nc.vector.tensor_scalar_max(z_relu[:, :], z[:, :], 0.0).then_inc(z_relu_done, 1)
                dve.wait_ge(z_relu_done, b + 1)
                nc.vector.tensor_scalar(l_part[:, :], g1_sb[:, 0, :], z_relu[:, 0:1], None, ALU.mult
                                        ).then_inc(l_part_done, 1)
                dve.wait_ge(l_part_done, b + 1)
                nc.vector.scalar_tensor_tensor(out=l_terms[:, :], in0=g1_sb[:, 1, :], scalar=z_relu[:, 1:2],
                                               in1=l_part[:, :], op0=ALU.mult, op1=ALU.add
                                               ).then_inc(l_terms_done, 1)
                if kind != "last":
                    hT_lo(b + 1)
                dve.wait_ge(logits_ready, b + 1)
                nc.vector.reduce_max(lmax[:, :], logits[:, :], AXIS.X).then_inc(max_done, 1)
                dve.wait_ge(max_done, b + 1)
                nc.vector.tensor_scalar(lshift[:, :], logits[:, :], lmax[:, :], None, ALU.subtract).then_inc(shift_done, 1)
                dve.wait_ge(exp_done, b + 1)
                nc.vector.reciprocal(lrec[:, :], lsum[:, :]).then_inc(rec_done, 1)
                dve.wait_ge(rec_done, b + 1)
                nc.vector.tensor_scalar(wgt[:, :], lexp[:, :], lrec[:, :], None, ALU.mult).then_inc(wgt_done, 1)
                dve.wait_ge(wgt_done, b + 1)
                dve.wait_ge(h_kept, b + 1)
                for c in range(SC):
                    dve.wait_ge(down_ready[c], b + 1)
                    nc.vector.scalar_tensor_tensor(out=part[:, c, :], in0=down[c][:, 0, :], scalar=wgt[:, 0:1],
                                                   in1=h_keep[:, c, :], op0=ALU.mult, op1=ALU.add
                                                   ).then_inc(part_done, 1)
                for c in range(SC):
                    dve.wait_ge(part_done, SC * b + c + 1)
                    wait(dve, out_stored[c], 16 * b)
                    nc.vector.scalar_tensor_tensor(out=out_sb[:, c, :], in0=down[c][:, 1, :], scalar=wgt[:, 1:2],
                                                   in1=part[:, c, :], op0=ALU.mult, op1=ALU.add
                                                   ).then_inc(final_done[c], 1)

            x_lo(0)
            for r in range(SC):
                dve.wait_ge(of_half(r, tT_hi_done), 1)
                nc.vector.tensor_tensor(rows0(tT_split, LO, r), turned_rows0(r), f32(rows0(tT_split, HI, r)),
                                        ALU.subtract).then_inc(of_half(r, tT_lo_done), 1)
            for r in range(SC):
                dve.wait_ge(of_half(r, h_ready), 1)
                nc.vector.tensor_tensor(h_sb[:, r], h_rows0[r][:, 0, :], x_sb[:, r], ALU.add
                                        ).then_inc(of_half(r, h_done), 1)
            piece_lo(0, 0)
            for r in range(SC):
                dve.wait_ge(of_half(r, hT_hi_done), 1)
                nc.vector.tensor_tensor(rows0(hT_split, LO, r), turned_rows0(r), f32(rows0(hT_split, HI, r)),
                                        ALU.subtract).then_inc(of_half(r, hT_lo_done), 1)
            piece_lo(0, 1)
            over_batches(dve, batch)

        @block.tensor
        def _(pe):
            def product_rows(dst, c):
                terms = [(j, l, r) for j in range(SC) for l, r in PASSES]
                for i, (j, l, r) in enumerate(terms):
                    last = nc.tensor.matmul(dst, tT_split[:, l, j, c * P:(c + 1) * P], x_split[:, r, j, :],
                                            start=i == 0, stop=i == len(terms) - 1)
                return last

            def h_product(b):
                pe.wait_ge(x_lo_done, b + 1)
                pe.wait_ge(tT_lo_done, b + 1)
                for c in range(SC):
                    last = product_rows(front[:, c, :], c)
                last.then_inc(h_ready, 1)

            def up_tile(kind, b, t):
                net, tt = divmod(t, TPN)
                wait(pe, prod_done, TILES * b + t - 1)
                for m, (bank, ready) in enumerate(((up_gate[t % 2], gate_ready), (up_lin[t % 2], lin_ready))):
                    if t % HALF_TILES == 0 and (net == EXPERT or kind == "first"):
                        pe.wait_ge(piece_split[2 * (tt // HALF_TILES) + m], b + 2 if net == EXPERT else 1)
                    for j in range(FPT):
                        f = tt * FPT + j
                        terms = [(c, l, r) for c in range(DC) for l, r in PASSES]
                        for i, (c, l, r) in enumerate(terms):
                            last = nc.tensor.matmul(bank[:, j, :], wi_split[m][:, net, l, c, f * P:(f + 1) * P],
                                                    hT_split[:, r, c, :], start=i == 0, stop=i == len(terms) - 1)
                    last.then_inc(ready, 1)

            def down_chunk(c, net):
                col = {EXPERT: 0, SHARED: 1}[net]
                terms = [(f, l, r) for f in range(FC) for l, r in PASSES]
                for i, (f, l, r) in enumerate(terms):
                    last = nc.tensor.matmul(down[c][:, col, :], prod_split[:, net, l, f, c * P:(c + 1) * P],
                                            wo_split[:, net, r, f, :], start=i == 0, stop=i == len(terms) - 1)
                return last

            def batch(kind, b):
                pe.wait_ge(hT_lo_done, b + 1)
                for t in range(TILES):
                    up_tile(kind, b, t)
                    if t == H_TILE and kind != "last":
                        h_product(b + 1)
                if kind == "first":
                    for k in WO:
                        pe.wait_ge(piece_split[k], 1)
                    pe.wait_ge(g0T_done, DC)
                pe.wait_ge(prod_lo_done, TILES * b + TPN)
                wait(pe, final_done[0], b)
                down_chunk(0, SHARED)
                pe.wait_ge(prod_lo_done, TILES * (b + 1))
                for k in WO:
                    pe.wait_ge(piece_split[k], b + 2)
                down_chunk(0, EXPERT).then_inc(down_ready[0], 1)
                wait(pe, final_done[1], b)
                down_chunk(1, SHARED)
                down_chunk(1, EXPERT).then_inc(down_ready[1], 1)

            def stay_warm(n):
                for _ in range(n):
                    nc.tensor.matmul(up_lin[1][:, 0, 0:P], ident[:, :], ident[:, :], start=True, stop=True)

            def turn_rows0(src, r, ready):
                for c in range(DC):
                    last = nc.tensor.transpose(turned0[r][:, 0, c * P:(c + 1) * P], src[:, r, c * P:(c + 1) * P],
                                               ident[:, :])
                last.then_inc(of_half(r, ready), 1)

            pe.wait_ge(ident_made, 1)
            stay_warm(FILL[0])
            for r in range(SC):
                pe.wait_ge(of_half(r, T_landed), 16)
                turn_rows0(T_sb, r, tT_ready)
            stay_warm(FILL[1])
            pe.wait_ge(x_lo_done, 1)
            for r in range(SC):
                pe.wait_ge(of_half(r, tT_lo_done), 1)
                product_rows(h_rows0[r][:, 0, :], r).then_inc(of_half(r, h_ready), 1)
            for r in range(SC):
                pe.wait_ge(of_half(r, h_done), 1)
                pe.wait_ge(of_half(r, tT_lo_done), 1)
                turn_rows0(h_sb, r, hT_ready)
            stay_warm(FILL[2])
            pe.wait_ge(g0_landed, 16)
            for m in range(DC):
                pe.wait_ge(h_done, 1)
                for c in range(2 * DC):
                    last = nc.tensor.transpose(g0T[m][:, c // 2, (c % 2) * P:(c % 2 + 1) * P],
                                               g0_sb[:, c, m * P:(m + 1) * P], ident[:, :])
                last.then_inc(g0T_ready, 1)
            pe.wait_ge(half[hT_lo_done], 1)
            over_batches(pe, batch)


_INS = ['x', 'itok_B_1_98', 'itok_B_0_2', 'L0_cond_T', 'L1_cond_Wi0', 'L1_cond_Wi1', 'L1_cond_Wo',
        'L1_cond_sWi0', 'L1_cond_sWi1', 'L1_cond_sWo', 'L1_cond_g0', 'L1_cond_g1']


def kernel(**inputs):
    import numpy as _np
    import concourse.bacc as _bacc
    from concourse import mybir as _mybir
    from concourse.bass_utils import run_bass_kernel_spmd as _run

    nc = _bacc.Bacc("TRN2", target_bir_lowering=False, num_devices=1)
    arrays, args = {}, []
    for name in _INS:
        a = _np.ascontiguousarray(inputs[name])
        arrays[f"in_{name}_dram"] = a
        args.append(nc.dram_tensor(f"in_{name}_dram", a.shape, _mybir.dt.from_np(a.dtype), kind="ExternalInput").ap())
    out = nc.dram_tensor("out_0_dram", inputs['x'].shape, _mybir.dt.float32, kind="ExternalOutput").ap()
    conditioned_residual_kernel(nc, *args, out)
    r = _run(nc, [arrays], core_ids=[0])
    return r.results[0]["out_0_dram"]
```
